# Optimizing a Trainium2 kernel written in Bass

```python
import numpy as np
import jax
import jax.numpy as jnp

def _softmax(x, axis=-1):
    return jax.nn.softmax(x, axis=axis)

def _gelu(x):
    return jax.nn.gelu(x, approximate=True)

def _silu(x):
    return jax.nn.silu(x)

def _sigmoid(x):
    return jax.nn.sigmoid(x)

def _layernorm(x, axis=-1, eps=1e-05):
    m = jnp.mean(x, axis=axis, keepdims=True)
    v = jnp.var(x, axis=axis, keepdims=True)
    return (x - m) / jnp.sqrt(v + eps)

def _scatter_add(tgt, idx, src, axis=0):
    return tgt.at[idx].add(src)

def _segment_sum(src, seg, n):
    return jax.ops.segment_sum(src, seg, n)
kernel_name = 'mk_adj_resnorm_d1_adj_r2_b98219'

def setup_inputs(seed: int=0):
    np.random.seed(seed)
    _w = jnp.asarray

    def _rec_inputs():
        import jax
        import jax.numpy as jnp
        _gk = jax.random.key(seed)
        x = -8.776e-05 + 1 * jax.random.normal(jax.random.fold_in(_gk, 1), (10000, 128), jnp.float32)
        _a = jax.random.bernoulli(jax.random.fold_in(_gk, 2), 0.0016, (10000, 10000))
        _a = jnp.logical_or(_a, jnp.eye(10000, dtype=bool))
        _af = _a.astype(jnp.float32)
        _af = _af * jax.random.uniform(jax.random.fold_in(_gk, 3), (10000, 10000), jnp.float32, 0.05, 1)
        adj = _af
        return (x, adj)
    x, adj = _rec_inputs()

    def _L0_gnn_setup():
        import jax, jax.numpy as jnp
        import numpy as np
        N_USER = 10000
        N_ITEM = 10000
        HID = 128
        key = jax.random.key(seed)
        k1, k2, k3, k4, k5, k6, k7 = jax.random.split(key, 7)
        scale = 1.0 / np.sqrt(HID)
        return {'user_feat': jax.random.normal(k1, (N_USER, HID), dtype=jnp.float32), 'item_feat': jax.random.normal(k2, (N_ITEM, HID), dtype=jnp.float32), 'adj': jax.random.uniform(k3, (N_USER, N_ITEM), dtype=jnp.float32), 'W_item': jax.random.uniform(k4, (HID, HID), dtype=jnp.float32, minval=-scale, maxval=scale), 'b_item': jax.random.uniform(k5, (HID,), dtype=jnp.float32, minval=-scale, maxval=scale), 'W_user': jax.random.uniform(k6, (HID, HID), dtype=jnp.float32, minval=-scale, maxval=scale), 'b_user': jax.random.uniform(k7, (HID,), dtype=jnp.float32, minval=-scale, maxval=scale)}
    _L0_gnn_all = _L0_gnn_setup()
    _L0_gnn_in = {k: v for k, v in _L0_gnn_all.items() if k in ('item_feat', 'W_item', 'b_item', 'W_user', 'b_user')}
    del _L0_gnn_all
    return {'x': x, 'adj': adj, 'L0_gnn_item_feat': _L0_gnn_in['item_feat'], 'L0_gnn_W_item': _L0_gnn_in['W_item'], 'L0_gnn_b_item': _L0_gnn_in['b_item'], 'L0_gnn_W_user': _L0_gnn_in['W_user'], 'L0_gnn_b_user': _L0_gnn_in['b_user']}

def reference(x, adj, L0_gnn_item_feat, L0_gnn_W_item, L0_gnn_b_item, L0_gnn_W_user, L0_gnn_b_user):
    import jax
    import jax.numpy as jnp

    def _L0_gnn_ref(user_feat, item_feat, adj, W_item, b_item, W_user, b_user):
        import jax, jax.numpy as jnp
        import numpy as np
        N_USER = 10000
        N_ITEM = 10000
        HID = 128
        h = item_feat @ W_item.T + b_item
        b = user_feat @ W_user.T + b_user
        return jax.nn.relu(adj @ h + b)
    x = _layernorm(x + _L0_gnn_ref(x, L0_gnn_item_feat, adj, L0_gnn_W_item, L0_gnn_b_item, L0_gnn_W_user, L0_gnn_b_user), axis=-1)
    return x

_drawn_inputs = setup_inputs


def setup_inputs(seed=0):
    import zlib

    import numpy as np

    out = dict(_drawn_inputs(seed))
    spreads = {}
    factors = {}
    for name, (base, spread) in spreads.items():
        noise = np.random.default_rng([zlib.crc32(name.encode()), seed]).standard_normal(out[name].shape)
        drawn = base * np.exp(spread * noise) if base else spread * noise
        out[name] = jnp.asarray(drawn.astype(out[name].dtype))
    for name, factor in factors.items():
        out[name] = (out[name] * factor).astype(out[name].dtype)
    return out
```

```python
from contextlib import ExitStack

import concourse.bass as bass
from concourse import mybir

F32 = mybir.dt.float32
ALU = mybir.AluOpType
ACT = mybir.ActivationFunctionType

P = 128
N_USER = 10000
N_ITEM = 10000
HID = 128
EPS = 1e-5

GROUP = 500
GROUPS = N_USER // GROUP
BLOCKS = 4
BLOCK = GROUP // BLOCKS
CHUNKS = N_ITEM // P
TAIL = N_ITEM - CHUNKS * P
PER_TILE = 5
TILES = -(-(CHUNKS + 2) // PER_TILE)
LAST_FULL = CHUNKS - (TILES - 1) * PER_TILE
RING = 4
ITEM_RING = 2
PAIRS = GROUPS // 2
TURN_TILE = 3
STORE_TILE = 12


def adj_count(g, t):
    per_group = 16 * (TILES // RING) + (16 if t % RING == RING - 1 else 0)
    return g * per_group + 16 * (t // RING + 1) + (16 if t == TILES - 1 else 0)


def later(g, n):
    return not isinstance(g, int) or g >= n


def gnn_kernel(nc, adj_t, adj_tail, x_t, item_t, w_item_t, b_item, w_user_t, b_user, out):
    with ExitStack() as ctx:
        def sb(name, shape, dt=F32):
            return ctx.enter_context(nc.sbuf_tensor(name, shape, dt))

        def psum(name, shape):
            return ctx.enter_context(nc.psum_tensor(name, shape, F32))

        def sem(name):
            return ctx.enter_context(nc.semaphore(name))

        adj = sb("adj", [P, RING, PER_TILE, GROUP])
        xg = sb("xg", [P, 2, GROUP])
        h = sb("h", [P, CHUNKS + 1, HID])
        items = sb("items", [P, ITEM_RING, PER_TILE * P])
        w_item = sb("w_item", [P, HID])
        w_user = sb("w_user", [P, HID])
        bias_item = sb("bias_item", [P, HID])
        bias_user = sb("bias_user", [P, 1])
        eps = sb("eps", [P, 1])
        ident = sb("ident", [P, P])
        relu_t = sb("relu_t", [P, GROUP])
        z_t = sb("z_t", [P, BLOCKS, P])
        stats = sb("stats", [P, BLOCKS, 6])
        moments = sb("moments", [P, BLOCKS, 2])
        std = sb("std", [P, BLOCKS])
        rstd = sb("rstd", [P, BLOCKS])
        normed = sb("normed", [P, 2, BLOCKS, HID])

        acc = [psum(f"acc{i}", [P, 512]) for i in range(2)]
        z_ps = psum("z_ps", [P, BLOCKS, HID])
        h_ps = [psum(f"h_ps{i}", [P, 8, HID]) for i in range(2)]

        adj_landed = [sem(f"adj_landed{i}") for i in range(RING)]
        x_landed = [sem(f"x_landed{i}") for i in range(2)]
        item_landed = [sem(f"item_landed{i}") for i in range(ITEM_RING)]
        weights_landed = sem("weights_landed")
        out_stored = [sem(f"out_stored{i}") for i in range(2)]
        ident_zeroed = sem("ident_zeroed")
        ident_ready = sem("ident_ready")
        pads_ready = sem("pads_ready")
        h_product = sem("h_product")
        h_ready = sem("h_ready")
        tile_done = sem("tile_done")
        acc_ready = sem("acc_ready")
        relu_done = sem("relu_done")
        z_added = sem("z_added")
        z_turned = sem("z_turned")
        stats_done = sem("stats_done")
        moments_done = sem("moments_done")
        std_done = sem("std_done")
        rstd_done = sem("rstd_done")
        out_ready = sem("out_ready")

        block = ctx.enter_context(nc.Block())

        def full_chunks(t):
            return PER_TILE if t < TILES - 1 else LAST_FULL

        @block.gpsimd
        def _(pool):
            nc.gpsimd.memset(ident[:, :], 0.0).then_inc(ident_zeroed, 1)
            pool.wait_ge(ident_zeroed, 1)
            nc.gpsimd.affine_select(out=ident[:, :], in_=ident[:, :], compare_op=ALU.not_equal, fill=1.0,
                                    base=0, pattern=[[-1, P]], channel_multiplier=1).then_inc(ident_ready, 1)

        @block.sync
        def _(sp):
            def load_items(t):
                if t >= ITEM_RING:
                    sp.wait_ge(h_product, t - ITEM_RING + 1)
                n = min(PER_TILE * P, N_ITEM - t * PER_TILE * P)
                sp.dma_start(items[:, t % ITEM_RING, 0:n],
                             item_t[:, t * PER_TILE * P:t * PER_TILE * P + n]).then_inc(item_landed[t % ITEM_RING], 16)

            def load_adj(g, t):
                if later(g, 1) or t >= RING:
                    sp.wait_ge(tile_done, g * TILES + t - RING + 1)
                n = full_chunks(t)
                sp.dma_start(adj[:, t % RING, 0:n, :],
                             adj_t[g, :, t * PER_TILE:t * PER_TILE + n, :]).then_inc(adj_landed[t % RING], 16)
                if t == TILES - 1:
                    sp.dma_start(adj[0:TAIL, t % RING, n, :], adj_tail[g]).then_inc(adj_landed[t % RING], 16)

            def load_x(g, parity):
                if later(g, 2):
                    sp.wait_ge(z_added, g - 1)
                sp.dma_start(xg[:, parity, :], x_t[g]).then_inc(x_landed[parity], 16)

            def store(g, parity):
                sp.wait_ge(out_ready, g + 1)
                sp.dma_start(out[g], normed[:, parity, :, :]).then_inc(out_stored[parity], 16)

            def load_group(g, parity):
                for t in range(TILES):
                    if t == STORE_TILE:
                        store(g - 1, 1 - parity)
                        load_x(g, parity)
                    load_adj(g, t)

            sp.dma_start(w_item[:, :], w_item_t).then_inc(weights_landed, 16)
            sp.dma_start(bias_item[:, :], b_item.rearrange("(a n) -> a n", a=1).to_broadcast([P, HID])).then_inc(weights_landed, 16)
            load_items(0)
            sp.dma_start(w_user[:, :], w_user_t).then_inc(weights_landed, 16)
            sp.dma_start(bias_user[:, :], b_user.rearrange("(p a) -> p a", a=1)).then_inc(weights_landed, 16)
            for t in range(TILES):
                if t + 1 < TILES:
                    load_items(t + 1)
                load_adj(0, t)
                if t == 4:
                    load_x(0, 0)
            load_group(1, 1)
            with sp.Fori(1, PAIRS) as i:
                load_group(2 * i, 0)
                load_group(2 * i + 1, 1)
            store(GROUPS - 1, 1)
            for parity in range(2):
                sp.wait_ge(out_stored[parity], 16 * (GROUPS // 2))

        @block.tensor
        def _(pe):
            def project_items(t):
                pe.wait_ge(item_landed[t % ITEM_RING], 16 * (t // ITEM_RING + 1))
                if t >= 2:
                    pe.wait_ge(h_ready, t - 1)
                n = full_chunks(t) + (1 if t == TILES - 1 else 0)
                for c in range(n):
                    m = min(P, N_ITEM - (t * PER_TILE + c) * P)
                    mm = nc.tensor.matmul(h_ps[t % 2][0:m, c, :], items[:, t % ITEM_RING, c * P:c * P + m],
                                          w_item[:, :], start=True, stop=True)
                mm.then_inc(h_product, 1)

            def tile_product(g, t, parity):
                pe.wait_ge(adj_landed[t % RING], adj_count(g, t))
                for c in range(full_chunks(t)):
                    mm = nc.tensor.matmul(acc[parity][:, 0:GROUP], h[:, t * PER_TILE + c, :],
                                          adj[:, t % RING, c, :], start=(t == 0 and c == 0), stop=False)
                if t == TILES - 1:
                    mm = nc.tensor.matmul(acc[parity][:, 0:GROUP], h[0:TAIL, CHUNKS, :],
                                          adj[0:TAIL, t % RING, LAST_FULL, :], start=False, stop=False)
                mm.then_inc(tile_done, 1)

            def user_product(half, parity):
                pe.wait_ge(x_landed[parity], 16 * (half + 1))
                nc.tensor.matmul(acc[parity][:, 0:GROUP], w_user[:, :], xg[:, parity, :],
                                 start=False, stop=True).then_inc(acc_ready, 1)

            def turn_back(g):
                pe.wait_ge(z_added, g + 1)
                for b in range(BLOCKS):
                    mm = nc.tensor.transpose(z_ps[:, b, :], z_t[:, b, :], ident[:, :])
                mm.then_inc(z_turned, 1)

            def group(g, half, parity):
                if later(g, 2):
                    pe.wait_ge(relu_done, g - 1)
                for t in range(TILES):
                    if t == TURN_TILE:
                        turn_back(g - 1)
                    tile_product(g, t, parity)
                user_product(half, parity)

            pe.wait_ge(weights_landed, 64)
            project_items(0)
            for t in range(TILES):
                if t + 1 < TILES:
                    project_items(t + 1)
                pe.wait_ge(h_ready, t + 1)
                tile_product(0, t, 0)
            user_product(0, 0)
            pe.wait_ge(ident_ready, 1)
            pe.wait_ge(pads_ready, 1)
            group(1, 0, 1)
            with pe.Fori(1, PAIRS) as i:
                group(2 * i, i, 0)
                group(2 * i + 1, i, 1)
            turn_back(GROUPS - 1)

        @block.scalar
        def _(act):
            def relu(g, parity):
                act.wait_ge(acc_ready, g + 1)
                if later(g, 1):
                    act.wait_ge(z_added, g)
                nc.scalar.activation(relu_t[:, :], acc[parity][:, 0:GROUP], ACT.Relu,
                                     bias=bias_user[:, 0:1]).then_inc(relu_done, 1)

            def deviation(g):
                act.wait_ge(moments_done, g + 1)
                nc.scalar.activation(std[:, :], moments[:, :, 1], ACT.Sqrt,
                                     bias=eps[:, 0:1]).then_inc(std_done, 1)

            act.wait_ge(weights_landed, 64)
            act.wait_ge(pads_ready, 1)
            def pair(i):
                for parity in range(2):
                    relu(2 * i + parity, parity)
                    deviation(2 * i + parity)

            pair(0)
            with act.Fori(1, PAIRS) as i:
                pair(i)

        @block.vector
        def _(dve):
            def add_item_bias(t):
                dve.wait_ge(h_product, t + 1)
                n = full_chunks(t)
                ins = nc.vector.tensor_tensor(h[:, t * PER_TILE:t * PER_TILE + n, :], h_ps[t % 2][:, 0:n, :],
                                              bias_item[:, None, :].to_broadcast([P, n, HID]), ALU.add)
                if t == TILES - 1:
                    ins = nc.vector.tensor_tensor(h[0:TAIL, CHUNKS, :], h_ps[t % 2][0:TAIL, n, :],
                                                  bias_item[0:TAIL, :], ALU.add)
                ins.then_inc(h_ready, 1)

            def add_x(g, half, parity):
                dve.wait_ge(relu_done, g + 1)
                dve.wait_ge(x_landed[parity], 16 * (half + 1))
                if later(g, 1):
                    dve.wait_ge(z_turned, g)
                nc.vector.tensor_tensor(z_t[:, :, 0:BLOCK],
                                        relu_t[:, :].rearrange("p (b n) -> p b n", b=BLOCKS),
                                        xg[:, parity, :].rearrange("p (b n) -> p b n", b=BLOCKS),
                                        ALU.add).then_inc(z_added, 1)

            def layernorm(g, half, parity):
                dve.wait_ge(z_turned, g + 1)
                for b in range(BLOCKS):
                    ins = nc.vector.bn_stats(stats[:, b, :], z_ps[:, b, :])
                ins.then_inc(stats_done, 1)
                dve.wait_ge(stats_done, g + 1)
                dve.nop(nofuse=True)
                for b in range(BLOCKS):
                    ins = nc.vector.bn_aggr(moments[:, b, :], stats[:, b, :])
                ins.then_inc(moments_done, 1)
                dve.wait_ge(std_done, g + 1)
                nc.vector.reciprocal(rstd[:, :], std[:, :]).then_inc(rstd_done, 1)
                dve.wait_ge(rstd_done, g + 1)
                if later(g, 2):
                    dve.wait_ge(out_stored[parity], 16 * half)
                for b in range(BLOCKS):
                    ins = nc.vector.tensor_scalar(normed[:, parity, b, :], z_ps[:, b, :],
                                                  moments[:, b, 0:1], rstd[:, b:b + 1],
                                                  ALU.subtract, ALU.mult)
                ins.then_inc(out_ready, 1)

            nc.vector.memset(eps[:, :], EPS)
            nc.vector.memset(z_t[:, :, :], 0.0).then_inc(pads_ready, 1)
            dve.wait_ge(weights_landed, 64)
            dve.wait_ge(pads_ready, 1)
            for t in range(TILES):
                add_item_bias(t)

            def pair(i):
                for parity in range(2):
                    add_x(2 * i + parity, i, parity)
                    layernorm(2 * i + parity, i, parity)

            pair(0)
            with dve.Fori(1, PAIRS) as i:
                pair(i)


def kernel(x, adj, L0_gnn_item_feat, L0_gnn_W_item, L0_gnn_b_item, L0_gnn_W_user, L0_gnn_b_user):
    import numpy as np
    import concourse.bacc as bacc
    from concourse.bass_utils import run_bass_kernel_spmd

    full = CHUNKS * P
    a = np.asarray(adj)
    groups = a.reshape(GROUPS, GROUP, N_ITEM)
    arrays = {
        "adj_t": np.ascontiguousarray(groups[:, :, :full].reshape(GROUPS, GROUP, CHUNKS, P).transpose(0, 3, 2, 1)),
        "adj_tail": np.ascontiguousarray(groups[:, :, full:].transpose(0, 2, 1)),
        "x_t": np.ascontiguousarray(np.asarray(x).reshape(GROUPS, GROUP, HID).transpose(0, 2, 1)),
        "item_t": np.ascontiguousarray(np.asarray(L0_gnn_item_feat).T),
        "w_item_t": np.ascontiguousarray(np.asarray(L0_gnn_W_item).T),
        "b_item": np.ascontiguousarray(L0_gnn_b_item),
        "w_user_t": np.ascontiguousarray(np.asarray(L0_gnn_W_user).T),
        "b_user": np.ascontiguousarray(L0_gnn_b_user),
    }
    nc = bacc.Bacc("TRN2", target_bir_lowering=False, num_devices=1)
    args = [nc.dram_tensor(n, v.shape, mybir.dt.from_np(v.dtype), kind="ExternalInput").ap() for n, v in arrays.items()]
    out = nc.dram_tensor("out", (GROUPS, P, BLOCKS, HID), F32, kind="ExternalOutput").ap()
    gnn_kernel(nc, *args, out)
    r = run_bass_kernel_spmd(nc, [arrays], core_ids=[0])
    got = r.results[0]["out"]
    return np.ascontiguousarray(got[:, :BLOCK].transpose(0, 2, 1, 3).reshape(N_USER, HID))
```

```python
from contextlib import ExitStack

import concourse.bass as bass
from concourse import mybir

F32 = mybir.dt.float32
F32R = mybir.dt.float32r
ALU = mybir.AluOpType
ACT = mybir.ActivationFunctionType

P = 128
N_USER = 10000
N_ITEM = 10000
HID = 128
EPS = 1e-5

GROUP = 500
GROUPS = N_USER // GROUP
BLOCKS = 4
BLOCK = GROUP // BLOCKS
FULL = N_ITEM // P
TAIL = N_ITEM - FULL * P
CHUNKS = FULL + 2
PER_TILE = 4
TILES = CHUNKS // PER_TILE
LAST = TILES - 1
LAST_FULL = FULL - LAST * PER_TILE
RING = 4
ITEM_RING = 2
H_RING = 3
PAIRS = GROUPS // 2

RELU_AT = 4
ADD_X_AT = 5
TURN_AT = 7
STATS_AT, MOMENTS_AT = 8, 9
STD_AT = 11
RSTD_AT, SHIFT_AT = 12, 13
NORM_AT = 15
LOAD_X_AT = 10
STORE_AT = 2


def later(g, n):
    return not isinstance(g, int) or g >= n


def adj_count(g, t):
    per_group = 16 * (TILES // RING) + (16 if t % RING == LAST % RING else 0)
    return g * per_group + 16 * (t // RING + 1) + (16 if t == LAST else 0)


def item_chunks(t):
    return PER_TILE if t < LAST else LAST_FULL + 1


def gnn_kernel(nc, adj_t, adj_tail, x_t, item_t, w_item_t, b_item, w_user_t, b_user, out):
    with ExitStack() as ctx:
        def sb(name, shape, dt=F32):
            return ctx.enter_context(nc.sbuf_tensor(name, shape, dt))

        def psum(name, shape):
            return ctx.enter_context(nc.psum_tensor(name, shape, F32))

        def sem(name):
            return ctx.enter_context(nc.semaphore(name))

        adj = sb("adj", [P, RING, PER_TILE, GROUP])
        adj_hi = sb("adj_hi", [P, RING, PER_TILE, GROUP], F32R)
        adj_lo = sb("adj_lo", [P, RING, PER_TILE, GROUP], F32R)
        xg = sb("xg", [P, GROUP])
        h_hi = sb("h_hi", [P, CHUNKS, HID], F32R)
        h_lo = sb("h_lo", [P, CHUNKS, HID], F32R)
        h_full = sb("h_full", [P, H_RING, PER_TILE, HID])
        items = sb("items", [P, ITEM_RING, PER_TILE * P])
        w_item = sb("w_item", [P, HID])
        w_user = sb("w_user", [P, HID])
        bias_item = sb("bias_item", [P, HID])
        bias_user = sb("bias_user", [P, 1])
        eps = sb("eps", [P, 1])
        ident = sb("ident", [P, P])
        relu_t = sb("relu_t", [P, GROUP])
        z_t = sb("z_t", [P, BLOCKS, P])
        stats = sb("stats", [P, BLOCKS, 6])
        moments = sb("moments", [P, BLOCKS, 2])
        std = sb("std", [P, BLOCKS])
        rstd = sb("rstd", [P, BLOCKS])
        shift = sb("shift", [P, BLOCKS])
        normed = sb("normed", [P, BLOCKS, HID])

        acc = [psum(f"acc{i}", [P, 512]) for i in range(2)]
        z_ps = psum("z_ps", [P, BLOCKS, HID])
        h_ps = [psum(f"h_ps{i}", [P, PER_TILE, HID]) for i in range(2)]

        adj_landed = [sem(f"adj_landed{i}") for i in range(RING)]
        item_landed = [sem(f"item_landed{i}") for i in range(ITEM_RING)]
        x_landed = sem("x_landed")
        weights_landed = sem("weights_landed")
        out_stored = sem("out_stored")
        ident_zeroed = sem("ident_zeroed")
        ident_ready = sem("ident_ready")
        pads_ready = sem("pads_ready")
        h_product = sem("h_product")
        tail_zeroed = sem("tail_zeroed")
        h_full_made = sem("h_full_made")
        w_hi_made = sem("w_hi_made")
        w_lo_made = sem("w_lo_made")
        h_hi_made = sem("h_hi_made")
        h_lo_made = sem("h_lo_made")
        hi_made = sem("hi_made")
        lo_made = sem("lo_made")
        tile_done = sem("tile_done")
        relu_done = sem("relu_done")
        z_added = sem("z_added")
        z_turned = sem("z_turned")
        stats_done = sem("stats_done")
        moments_done = sem("moments_done")
        std_done = sem("std_done")
        rstd_done = sem("rstd_done")
        shift_done = sem("shift_done")
        out_ready = sem("out_ready")

        block = ctx.enter_context(nc.Block())

        @block.sync
        def _(sp):
            def load_items(t):
                if t >= ITEM_RING:
                    sp.wait_ge(h_product, t - ITEM_RING + 1)
                n = min(PER_TILE * P, N_ITEM - t * PER_TILE * P)
                sp.dma_start(items[:, t % ITEM_RING, 0:n],
                             item_t[:, t * PER_TILE * P:t * PER_TILE * P + n]).then_inc(item_landed[t % ITEM_RING], 16)

            def load_adj(g, t):
                if later(g, 1) or t >= RING:
                    sp.wait_ge(lo_made, g * TILES + t - RING + 1)
                n = PER_TILE if t < LAST else LAST_FULL
                sp.dma_start(adj[:, t % RING, 0:n, :],
                             adj_t[g, :, t * PER_TILE:t * PER_TILE + n, :]).then_inc(adj_landed[t % RING], 16)
                if t == LAST:
                    sp.dma_start(adj[0:TAIL, t % RING, n, :], adj_tail[g]).then_inc(adj_landed[t % RING], 16)

            def load_x(g):
                if later(g, 1):
                    sp.wait_ge(z_added, g)
                sp.dma_start(xg[:, :], x_t[g]).then_inc(x_landed, 16)

            def store(g):
                sp.wait_ge(out_ready, g + 1)
                sp.dma_start(out[g], normed[:, :, :]).then_inc(out_stored, 16)

            def load_group(g):
                for t in range(TILES):
                    if t == STORE_AT and later(g, 2):
                        store(g - 2)
                    if t == LOAD_X_AT:
                        load_x(g)
                    load_adj(g, t)

            sp.dma_start(w_item[:, :], w_item_t).then_inc(weights_landed, 16)
            load_items(0)
            sp.dma_start(bias_item[:, :], b_item.rearrange("(a n) -> a n", a=1).to_broadcast([P, HID])).then_inc(weights_landed, 16)
            load_items(1)
            sp.dma_start(w_user[:, :], w_user_t).then_inc(weights_landed, 16)
            sp.dma_start(bias_user[:, :], b_user.rearrange("(p a) -> p a", a=1)).then_inc(weights_landed, 16)
            for t in range(TILES):
                if t >= ITEM_RING:
                    load_items(t)
                if t == LOAD_X_AT:
                    load_x(0)
                load_adj(0, t)
            load_group(1)
            with sp.Fori(1, PAIRS) as i:
                load_group(2 * i)
                load_group(2 * i + 1)
            store(GROUPS - 2)
            store(GROUPS - 1)
            sp.wait_ge(out_stored, 16 * GROUPS)

        @block.tensor
        def _(pe):
            def project_items(t):
                pe.wait_ge(item_landed[t % ITEM_RING], 16 * (t // ITEM_RING + 1))
                if t >= 2:
                    pe.wait_ge(h_full_made, t - 1)
                for c in range(item_chunks(t)):
                    m = min(P, N_ITEM - (t * PER_TILE + c) * P)
                    mm = nc.tensor.matmul(h_ps[t % 2][0:m, c, :], items[:, t % ITEM_RING, c * P:c * P + m],
                                          w_item[:, :], start=True, stop=True)
                mm.then_inc(h_product, 1)

            def tile_product(g, t, parity):
                pe.wait_ge(lo_made, g * TILES + t + 1)
                s = t % RING
                for c in range(PER_TILE):
                    k = t * PER_TILE + c
                    into = acc[parity][:, 0:GROUP]
                    nc.tensor.matmul(into, h_hi[:, k, :], adj_hi[:, s, c, :], start=(k == 0), stop=False)
                    nc.tensor.matmul(into, h_hi[:, k, :], adj_lo[:, s, c, :], start=False, stop=False)
                    mm = nc.tensor.matmul(into, h_lo[:, k, :], adj_hi[:, s, c, :],
                                          start=False, stop=(k == CHUNKS - 1))
                mm.then_inc(tile_done, 1)

            def turn_back(g):
                pe.wait_ge(z_added, g + 1)
                if later(g, 1):
                    pe.wait_ge(out_ready, g)
                for b in range(BLOCKS):
                    mm = nc.tensor.transpose(z_ps[:, b, :], z_t[:, b, :], ident[:, :])
                mm.then_inc(z_turned, 1)

            def group(g, parity):
                if later(g, 2):
                    pe.wait_ge(relu_done, g - 1)
                for t in range(TILES):
                    if t == TURN_AT:
                        turn_back(g - 1)
                    tile_product(g, t, parity)

            pe.wait_ge(weights_landed, 64)
            project_items(0)
            project_items(1)
            for t in range(TILES):
                if t + 2 < TILES:
                    project_items(t + 2)
                if t == LAST:
                    pe.wait_ge(w_lo_made, 1)
                pe.wait_ge(h_lo_made, t + 1)
                tile_product(0, t, 0)
            pe.wait_ge(ident_ready, 1)
            pe.wait_ge(pads_ready, 1)
            group(1, 1)
            with pe.Fori(1, PAIRS) as i:
                group(2 * i, 0)
                group(2 * i + 1, 1)
            turn_back(GROUPS - 1)

        @block.scalar
        def _(act):
            def split_hi(g, t):
                s = t % RING
                n = item_chunks(t)
                act.wait_ge(adj_landed[s], adj_count(g, t))
                if later(g, 1) or t >= RING:
                    act.wait_ge(tile_done, g * TILES + t - RING + 1)
                ins = nc.scalar.copy(adj_hi[:, s, 0:n, :], adj[:, s, 0:n, :])
                if t == LAST:
                    act.wait_ge(x_landed, 16 * (g + 1))
                    ins = nc.scalar.copy(adj_hi[:, s, n, :], xg[:, :])
                ins.then_inc(hi_made, 1)

            def relu(g, parity):
                act.wait_ge(tile_done, (g + 1) * TILES)
                if later(g, 1):
                    act.wait_ge(z_added, g)
                nc.scalar.activation(relu_t[:, :], acc[parity][:, 0:GROUP], ACT.Relu,
                                     bias=bias_user[:, 0:1]).then_inc(relu_done, 1)

            def deviation(g):
                act.wait_ge(moments_done, g + 1)
                nc.scalar.activation(std[:, :], moments[:, :, 1], ACT.Sqrt, bias=eps[:, 0:1]).then_inc(std_done, 1)

            def normalise(g):
                act.wait_ge(shift_done, g + 1)
                if later(g, 1):
                    act.wait_ge(out_stored, 16 * g)
                for b in range(BLOCKS):
                    ins = nc.scalar.activation(normed[:, b, :], z_ps[:, b, :], ACT.Identity,
                                               bias=shift[:, b:b + 1], scale=rstd[:, b:b + 1])
                ins.then_inc(out_ready, 1)

            def group(g, parity):
                for t in range(TILES):
                    split_hi(g, t)
                    if t == RELU_AT:
                        relu(g - 1, 1 - parity)
                    if t == STD_AT:
                        deviation(g - 1)
                    if t == NORM_AT:
                        normalise(g - 1)

            
            act.wait_ge(weights_landed, 64)
            nc.scalar.copy(h_hi[:, CHUNKS - 1, :], w_user[:, :]).then_inc(w_hi_made, 1)
            act.wait_ge(pads_ready, 1)
            for t in range(TILES):
                split_hi(0, t)
                act.wait_ge(h_full_made, t + 1)
                n = item_chunks(t)
                nc.scalar.copy(h_hi[:, t * PER_TILE:t * PER_TILE + n, :],
                               h_full[:, t % H_RING, 0:n, :]).then_inc(h_hi_made, 1)
            group(1, 1)
            with act.Fori(1, PAIRS) as i:
                group(2 * i, 0)
                group(2 * i + 1, 1)
            relu(GROUPS - 1, 1)
            deviation(GROUPS - 1)
            normalise(GROUPS - 1)

        @block.gpsimd
        def _(pool):
            nc.gpsimd.memset(ident[:, :], 0.0).then_inc(ident_zeroed, 1)
            pool.wait_ge(ident_zeroed, 1)
            nc.gpsimd.affine_select(out=ident[:, :], in_=ident[:, :], compare_op=ALU.not_equal, fill=1.0,
                                    base=0, pattern=[[-1, P]], channel_multiplier=1).then_inc(ident_ready, 1)
            pool.wait_ge(w_hi_made, 1)
            nc.gpsimd.tensor_tensor(h_lo[:, CHUNKS - 1, :], w_user[:, :], h_hi[:, CHUNKS - 1, :].bitcast(F32),
                                    ALU.subtract).then_inc(w_lo_made, 1)
            for t in range(TILES):
                n = item_chunks(t)
                k = t * PER_TILE
                pool.wait_ge(h_hi_made, t + 1)
                nc.gpsimd.tensor_tensor(h_lo[:, k:k + n, :], h_full[:, t % H_RING, 0:n, :],
                                        h_hi[:, k:k + n, :].bitcast(F32), ALU.subtract).then_inc(h_lo_made, 1)

        @block.vector
        def _(dve):
            def add_item_bias(t):
                n = item_chunks(t)
                s = t % H_RING
                if t >= H_RING:
                    dve.wait_ge(h_lo_made, t - H_RING + 1)
                if t == LAST:
                    n -= 1
                    nc.vector.memset(h_full[:, s, n, :], 0.0).then_inc(tail_zeroed, 1)
                    dve.wait_ge(tail_zeroed, 1)
                dve.wait_ge(h_product, t + 1)
                ins = nc.vector.tensor_tensor(h_full[:, s, 0:n, :], h_ps[t % 2][:, 0:n, :],
                                              bias_item[:, None, :].to_broadcast([P, n, HID]), ALU.add)
                if t == LAST:
                    ins = nc.vector.tensor_tensor(h_full[0:TAIL, s, n, :], h_ps[t % 2][0:TAIL, n, :],
                                                  bias_item[0:TAIL, :], ALU.add)
                ins.then_inc(h_full_made, 1)

            def split_lo(g, t):
                s = t % RING
                n = item_chunks(t)
                dve.wait_ge(hi_made, g * TILES + t + 1)
                ins = nc.vector.tensor_tensor(adj_lo[:, s, 0:n, :], adj[:, s, 0:n, :],
                                              adj_hi[:, s, 0:n, :].bitcast(F32), ALU.subtract)
                if t == LAST:
                    ins = nc.vector.tensor_tensor(adj_lo[:, s, n, :], xg[:, :],
                                                  adj_hi[:, s, n, :].bitcast(F32), ALU.subtract)
                ins.then_inc(lo_made, 1)

            def add_x(g):
                dve.wait_ge(relu_done, g + 1)
                if later(g, 1):
                    dve.wait_ge(z_turned, g)
                nc.vector.tensor_tensor(z_t[:, :, 0:BLOCK],
                                        relu_t[:, :].rearrange("p (b n) -> p b n", b=BLOCKS),
                                        xg[:, :].rearrange("p (b n) -> p b n", b=BLOCKS),
                                        ALU.add).then_inc(z_added, 1)

            def statistics(g):
                dve.wait_ge(z_turned, g + 1)
                for b in range(BLOCKS):
                    ins = nc.vector.bn_stats(stats[:, b, :], z_ps[:, b, :])
                ins.then_inc(stats_done, 1)

            def aggregate(g):
                if later(g, 1):
                    dve.wait_ge(out_ready, g)
                dve.wait_ge(stats_done, g + 1)
                dve.nop(nofuse=True)
                for b in range(BLOCKS):
                    ins = nc.vector.bn_aggr(moments[:, b, :], stats[:, b, :])
                ins.then_inc(moments_done, 1)

            def reciprocal(g):
                dve.wait_ge(std_done, g + 1)
                nc.vector.reciprocal(rstd[:, :], std[:, :]).then_inc(rstd_done, 1)

            def mean_shift(g):
                dve.wait_ge(rstd_done, g + 1)
                nc.vector.scalar_tensor_tensor(out=shift[:, :], in0=moments[:, :, 0], scalar=-1.0,
                                               in1=rstd[:, :], op0=ALU.mult, op1=ALU.mult).then_inc(shift_done, 1)

            def group(g):
                for t in range(TILES):
                    split_lo(g, t)
                    if t == ADD_X_AT:
                        add_x(g - 1)
                    if t == STATS_AT:
                        statistics(g - 1)
                    if t == MOMENTS_AT:
                        aggregate(g - 1)
                    if t == RSTD_AT:
                        reciprocal(g - 1)
                    if t == SHIFT_AT:
                        mean_shift(g - 1)

            nc.vector.memset(eps[:, :], EPS)
            nc.vector.memset(z_t[:, :, :], 0.0).then_inc(pads_ready, 1)
            dve.wait_ge(pads_ready, 1)
            dve.wait_ge(weights_landed, 64)
            add_item_bias(0)
            add_item_bias(1)
            for t in range(TILES):
                split_lo(0, t)
                if t + 2 < TILES:
                    add_item_bias(t + 2)
            group(1)
            with dve.Fori(1, PAIRS) as i:
                group(2 * i)
                group(2 * i + 1)
            add_x(GROUPS - 1)
            statistics(GROUPS - 1)
            aggregate(GROUPS - 1)
            reciprocal(GROUPS - 1)
            mean_shift(GROUPS - 1)


def kernel(x, adj, L0_gnn_item_feat, L0_gnn_W_item, L0_gnn_b_item, L0_gnn_W_user, L0_gnn_b_user):
    import numpy as np
    import concourse.bacc as bacc
    from concourse.bass_utils import run_bass_kernel_spmd

    full = FULL * P
    groups = np.asarray(adj).reshape(GROUPS, GROUP, N_ITEM)
    arrays = {
        "adj_t": np.ascontiguousarray(groups[:, :, :full].reshape(GROUPS, GROUP, FULL, P).transpose(0, 3, 2, 1)),
        "adj_tail": np.ascontiguousarray(groups[:, :, full:].transpose(0, 2, 1)),
        "x_t": np.ascontiguousarray(np.asarray(x).reshape(GROUPS, GROUP, HID).transpose(0, 2, 1)),
        "item_t": np.ascontiguousarray(np.asarray(L0_gnn_item_feat).T),
        "w_item_t": np.ascontiguousarray(np.asarray(L0_gnn_W_item).T),
        "b_item": np.ascontiguousarray(L0_gnn_b_item),
        "w_user_t": np.ascontiguousarray(np.asarray(L0_gnn_W_user).T),
        "b_user": np.ascontiguousarray(L0_gnn_b_user),
    }
    nc = bacc.Bacc("TRN2", target_bir_lowering=False, num_devices=1)
    args = [nc.dram_tensor(n, v.shape, mybir.dt.from_np(v.dtype), kind="ExternalInput").ap() for n, v in arrays.items()]
    out = nc.dram_tensor("out", (GROUPS, P, BLOCKS, HID), F32, kind="ExternalOutput").ap()
    gnn_kernel(nc, *args, out)
    r = run_bass_kernel_spmd(nc, [arrays], core_ids=[0])
    got = r.results[0]["out"]
    return np.ascontiguousarray(got[:, :BLOCK].transpose(0, 2, 1, 3).reshape(N_USER, HID))
```

```python
from contextlib import ExitStack

import concourse.bass as bass
from concourse import mybir

F32 = mybir.dt.float32
F32R = mybir.dt.float32r
ALU = mybir.AluOpType
ACT = mybir.ActivationFunctionType

P = 128
N_USER = 10000
N_ITEM = 10000
HID = 128
EPS = 1e-5

GROUP = 500
GROUPS = N_USER // GROUP
BLOCKS = 4
BLOCK = GROUP // BLOCKS
FULL = N_ITEM // P
TAIL = N_ITEM - FULL * P
CHUNKS = FULL + 2
PER_TILE = 4
TILES = CHUNKS // PER_TILE
LAST = TILES - 1
LAST_FULL = FULL - LAST * PER_TILE
AT_TAIL, AT_USER, AT_FULL = 0, 1, 2
STEPS = TILES + 1
ADJ_RING = 5
PART_RING = 4
ITEM_RING = 2
H_RING = 3
PAIRS = GROUPS // 2

RELU_AT = 4
ADD_X_AT = 5
TURN_AT = 7
STATS_AT, MOMENTS_AT = 8, 9
STD_AT = 11
RSTD_AT, SHIFT_AT = 12, 13
NORM_AT = 15
LOAD_X_AT = 10
STORE_AT = 2


def later(g, n):
    return not isinstance(g, int) or g >= n


def adj_count(g, t):
    return g * 16 * (TILES // ADJ_RING) + 16 * (t // ADJ_RING + 1)


def steps_to(g, t):
    if t < 0:
        return steps_to(g - 1, TILES + t)
    return g * STEPS + t + 1 + (1 if t == LAST else 0)


def item_chunks(t):
    return PER_TILE if t < LAST else LAST_FULL + 1


def chunk(t, c):
    if t < LAST:
        return t * PER_TILE + c
    return {AT_TAIL: FULL, AT_USER: FULL + 1}.get(c, t * PER_TILE + c - AT_FULL)


def gnn_kernel(nc, adj_t, adj_tail, x_t, item_t, w_item_t, b_item, w_user_t, b_user, out):
    with ExitStack() as ctx:
        def sb(name, shape, dt=F32):
            return ctx.enter_context(nc.sbuf_tensor(name, shape, dt))

        def psum(name, shape):
            return ctx.enter_context(nc.psum_tensor(name, shape, F32))

        def sem(name):
            return ctx.enter_context(nc.semaphore(name))

        adj = sb("adj", [P, ADJ_RING, PER_TILE, GROUP])
        adj_hi = sb("adj_hi", [P, PART_RING, PER_TILE, GROUP], F32R)
        adj_lo = sb("adj_lo", [P, PART_RING, PER_TILE, GROUP], F32R)
        xg = sb("xg", [P, GROUP])
        h_hi = sb("h_hi", [P, CHUNKS, HID], F32R)
        h_lo = sb("h_lo", [P, CHUNKS, HID], F32R)
        h_full = sb("h_full", [P, H_RING, PER_TILE, HID])
        items = sb("items", [P, ITEM_RING, PER_TILE * P])
        w_item = sb("w_item", [P, HID])
        w_user = sb("w_user", [P, HID])
        bias_item = sb("bias_item", [P, HID])
        bias_user = sb("bias_user", [P, 1])
        eps = sb("eps", [P, 1])
        ident = sb("ident", [P, P])
        relu_t = sb("relu_t", [P, GROUP])
        z_t = sb("z_t", [P, BLOCKS, P])
        stats = sb("stats", [P, BLOCKS, 6])
        moments = sb("moments", [P, BLOCKS, 2])
        std = sb("std", [P, BLOCKS])
        rstd = sb("rstd", [P, BLOCKS])
        shift = sb("shift", [P, BLOCKS])
        normed = sb("normed", [P, BLOCKS, HID])

        acc = [psum(f"acc{i}", [P, 512]) for i in range(2)]
        z_ps = psum("z_ps", [P, BLOCKS, HID])
        h_ps = [psum(f"h_ps{i}", [P, PER_TILE, HID]) for i in range(2)]

        adj_landed = [sem(f"adj_landed{i}") for i in range(ADJ_RING)]
        item_landed = [sem(f"item_landed{i}") for i in range(ITEM_RING)]
        tail_landed = sem("tail_landed")
        x_landed = sem("x_landed")
        weights_landed = sem("weights_landed")
        out_stored = sem("out_stored")
        ident_zeroed = sem("ident_zeroed")
        ident_ready = sem("ident_ready")
        pads_ready = sem("pads_ready")
        h_product = sem("h_product")
        tail_zeroed = sem("tail_zeroed")
        h_full_made = sem("h_full_made")
        w_hi_made = sem("w_hi_made")
        w_lo_made = sem("w_lo_made")
        h_hi_made = sem("h_hi_made")
        h_lo_made = sem("h_lo_made")
        hi_made = sem("hi_made")
        lo_made = sem("lo_made")
        tile_done = sem("tile_done")
        relu_done = sem("relu_done")
        z_added = sem("z_added")
        z_turned = sem("z_turned")
        stats_done = sem("stats_done")
        moments_done = sem("moments_done")
        std_done = sem("std_done")
        rstd_done = sem("rstd_done")
        shift_done = sem("shift_done")
        out_ready = sem("out_ready")

        block = ctx.enter_context(nc.Block())

        @block.sync
        def _(sp):
            def load_items(t):
                if t >= ITEM_RING:
                    sp.wait_ge(h_product, t - ITEM_RING + 1)
                n = min(PER_TILE * P, N_ITEM - t * PER_TILE * P)
                sp.dma_start(items[:, t % ITEM_RING, 0:n],
                             item_t[:, t * PER_TILE * P:t * PER_TILE * P + n]).then_inc(item_landed[t % ITEM_RING], 16)

            def load_adj(g, t):
                if later(g, 1) or t >= ADJ_RING:
                    sp.wait_ge(lo_made, steps_to(g, t - ADJ_RING))
                n = PER_TILE if t < LAST else LAST_FULL
                if t == LAST:
                    sp.dma_start(adj[0:TAIL, t % ADJ_RING, AT_TAIL, :], adj_tail[g]).then_inc(tail_landed, 16)
                sp.dma_start(adj[:, t % ADJ_RING, PER_TILE - n:PER_TILE, :],
                             adj_t[g, :, t * PER_TILE:t * PER_TILE + n, :]).then_inc(adj_landed[t % ADJ_RING], 16)

            def load_x(g):
                if later(g, 1):
                    sp.wait_ge(z_added, g)
                sp.dma_start(xg[:, :], x_t[g]).then_inc(x_landed, 16)

            def store(g):
                sp.wait_ge(out_ready, g + 1)
                sp.dma_start(out[g], normed[:, :, :]).then_inc(out_stored, 16)

            def load_group(g):
                for t in range(TILES):
                    if t == STORE_AT and later(g, 2):
                        store(g - 2)
                    if t == LOAD_X_AT:
                        load_x(g)
                    load_adj(g, t)

            sp.dma_start(w_item[:, :], w_item_t).then_inc(weights_landed, 16)
            load_items(0)
            sp.dma_start(bias_item[:, :], b_item.rearrange("(a n) -> a n", a=1).to_broadcast([P, HID])).then_inc(weights_landed, 16)
            load_items(1)
            sp.dma_start(w_user[:, :], w_user_t).then_inc(weights_landed, 16)
            sp.dma_start(bias_user[:, :], b_user.rearrange("(p a) -> p a", a=1)).then_inc(weights_landed, 16)
            for t in range(TILES):
                if t >= ITEM_RING:
                    load_items(t)
                if t == LOAD_X_AT:
                    load_x(0)
                load_adj(0, t)
            load_group(1)
            with sp.Fori(1, PAIRS) as i:
                load_group(2 * i)
                load_group(2 * i + 1)
            store(GROUPS - 2)
            store(GROUPS - 1)
            sp.wait_ge(out_stored, 16 * GROUPS)

        @block.tensor
        def _(pe):
            def project_items(t):
                pe.wait_ge(item_landed[t % ITEM_RING], 16 * (t // ITEM_RING + 1))
                if t >= 2:
                    pe.wait_ge(h_full_made, t - 1)
                for c in range(item_chunks(t)):
                    m = min(P, N_ITEM - (t * PER_TILE + c) * P)
                    mm = nc.tensor.matmul(h_ps[t % 2][0:m, c, :], items[:, t % ITEM_RING, c * P:c * P + m],
                                          w_item[:, :], start=True, stop=True)
                mm.then_inc(h_product, 1)

            def tile_product(g, t, parity):
                s = t % PART_RING
                into = acc[parity][:, 0:GROUP]
                parts = [(range(PER_TILE), steps_to(g, t))]
                if t == LAST:
                    parts = [(range(AT_FULL), steps_to(g, t) - 1), (range(AT_FULL, PER_TILE), steps_to(g, t))]
                for places, steps in parts:
                    pe.wait_ge(hi_made, steps)
                    for c in places:
                        k = chunk(t, c)
                        nc.tensor.matmul(into, h_hi[:, k, :], adj_hi[:, s, c, :], start=(k == 0), stop=False)
                        nc.tensor.matmul(into, h_lo[:, k, :], adj_hi[:, s, c, :], start=False, stop=False)
                    pe.wait_ge(lo_made, steps)
                    for c in places:
                        mm = nc.tensor.matmul(into, h_hi[:, chunk(t, c), :], adj_lo[:, s, c, :],
                                              start=False, stop=(t == LAST and c == PER_TILE - 1))
                mm.then_inc(tile_done, 1)

            def turn_back(g):
                pe.wait_ge(z_added, g + 1)
                if later(g, 1):
                    pe.wait_ge(out_ready, g)
                for b in range(BLOCKS):
                    mm = nc.tensor.transpose(z_ps[:, b, :], z_t[:, b, :], ident[:, :])
                mm.then_inc(z_turned, 1)

            def group(g, parity):
                if later(g, 2):
                    pe.wait_ge(relu_done, g - 1)
                for t in range(TILES):
                    if t == TURN_AT:
                        turn_back(g - 1)
                    tile_product(g, t, parity)

            pe.wait_ge(weights_landed, 64)
            project_items(0)
            project_items(1)
            for t in range(TILES):
                if t + 2 < TILES:
                    project_items(t + 2)
                if t == LAST:
                    pe.wait_ge(w_lo_made, 1)
                pe.wait_ge(h_lo_made, t + 1)
                tile_product(0, t, 0)
            pe.wait_ge(ident_ready, 1)
            pe.wait_ge(pads_ready, 1)
            group(1, 1)
            with pe.Fori(1, PAIRS) as i:
                group(2 * i, 0)
                group(2 * i + 1, 1)
            turn_back(GROUPS - 1)

        @block.scalar
        def _(act):
            def split_hi(g, t):
                a, s = t % ADJ_RING, t % PART_RING
                start = 0
                if later(g, 1) or t >= PART_RING:
                    act.wait_ge(tile_done, g * TILES + t - PART_RING + 1)
                if t == LAST:
                    act.wait_ge(tail_landed, 16 * (g + 1))
                    nc.scalar.copy(adj_hi[:, s, AT_TAIL, :], adj[:, a, AT_TAIL, :])
                    act.wait_ge(x_landed, 16 * (g + 1))
                    nc.scalar.copy(adj_hi[:, s, AT_USER, :], xg[:, :]).then_inc(hi_made, 1)
                    start = AT_FULL
                act.wait_ge(adj_landed[a], adj_count(g, t))
                nc.scalar.copy(adj_hi[:, s, start:, :], adj[:, a, start:, :]).then_inc(hi_made, 1)

            def relu(g, parity):
                act.wait_ge(tile_done, (g + 1) * TILES)
                if later(g, 1):
                    act.wait_ge(z_added, g)
                nc.scalar.activation(relu_t[:, :], acc[parity][:, 0:GROUP], ACT.Relu,
                                     bias=bias_user[:, 0:1]).then_inc(relu_done, 1)

            def deviation(g):
                act.wait_ge(moments_done, g + 1)
                nc.scalar.activation(std[:, :], moments[:, :, 1], ACT.Sqrt, bias=eps[:, 0:1]).then_inc(std_done, 1)

            def normalise(g):
                act.wait_ge(shift_done, g + 1)
                if later(g, 1):
                    act.wait_ge(out_stored, 16 * g)
                for b in range(BLOCKS):
                    ins = nc.scalar.activation(normed[:, b, :], z_ps[:, b, :], ACT.Identity,
                                               bias=shift[:, b:b + 1], scale=rstd[:, b:b + 1])
                ins.then_inc(out_ready, 1)

            def group(g, parity):
                for t in range(TILES):
                    split_hi(g, t)
                    if t == RELU_AT:
                        relu(g - 1, 1 - parity)
                    if t == STD_AT:
                        deviation(g - 1)
                    if t == NORM_AT:
                        normalise(g - 1)

            
            act.wait_ge(weights_landed, 64)
            nc.scalar.copy(h_hi[:, CHUNKS - 1, :], w_user[:, :]).then_inc(w_hi_made, 1)
            act.wait_ge(pads_ready, 1)
            for t in range(TILES):
                split_hi(0, t)
                act.wait_ge(h_full_made, t + 1)
                n = item_chunks(t)
                nc.scalar.copy(h_hi[:, t * PER_TILE:t * PER_TILE + n, :],
                               h_full[:, t % H_RING, 0:n, :]).then_inc(h_hi_made, 1)
            group(1, 1)
            with act.Fori(1, PAIRS) as i:
                group(2 * i, 0)
                group(2 * i + 1, 1)
            relu(GROUPS - 1, 1)
            deviation(GROUPS - 1)
            normalise(GROUPS - 1)

        @block.gpsimd
        def _(pool):
            nc.gpsimd.memset(ident[:, :], 0.0).then_inc(ident_zeroed, 1)
            pool.wait_ge(ident_zeroed, 1)
            nc.gpsimd.affine_select(out=ident[:, :], in_=ident[:, :], compare_op=ALU.not_equal, fill=1.0,
                                    base=0, pattern=[[-1, P]], channel_multiplier=1).then_inc(ident_ready, 1)
            pool.wait_ge(w_hi_made, 1)
            nc.gpsimd.tensor_tensor(h_lo[:, CHUNKS - 1, :], w_user[:, :], h_hi[:, CHUNKS - 1, :].bitcast(F32),
                                    ALU.subtract).then_inc(w_lo_made, 1)
            for t in range(TILES):
                n = item_chunks(t)
                k = t * PER_TILE
                pool.wait_ge(h_hi_made, t + 1)
                nc.gpsimd.tensor_tensor(h_lo[:, k:k + n, :], h_full[:, t % H_RING, 0:n, :],
                                        h_hi[:, k:k + n, :].bitcast(F32), ALU.subtract).then_inc(h_lo_made, 1)

        @block.vector
        def _(dve):
            def add_item_bias(t):
                n = item_chunks(t)
                s = t % H_RING
                if t >= H_RING:
                    dve.wait_ge(h_lo_made, t - H_RING + 1)
                if t == LAST:
                    n -= 1
                    nc.vector.memset(h_full[:, s, n, :], 0.0).then_inc(tail_zeroed, 1)
                    dve.wait_ge(tail_zeroed, 1)
                dve.wait_ge(h_product, t + 1)
                ins = nc.vector.tensor_tensor(h_full[:, s, 0:n, :], h_ps[t % 2][:, 0:n, :],
                                              bias_item[:, None, :].to_broadcast([P, n, HID]), ALU.add)
                if t == LAST:
                    ins = nc.vector.tensor_tensor(h_full[0:TAIL, s, n, :], h_ps[t % 2][0:TAIL, n, :],
                                                  bias_item[0:TAIL, :], ALU.add)
                ins.then_inc(h_full_made, 1)

            def split_lo(g, t):
                a, s = t % ADJ_RING, t % PART_RING
                start = 0
                if t == LAST:
                    dve.wait_ge(hi_made, steps_to(g, t) - 1)
                    nc.vector.tensor_tensor(adj_lo[:, s, AT_TAIL, :], adj[:, a, AT_TAIL, :],
                                            adj_hi[:, s, AT_TAIL, :].bitcast(F32), ALU.subtract)
                    nc.vector.tensor_tensor(adj_lo[:, s, AT_USER, :], xg[:, :],
                                            adj_hi[:, s, AT_USER, :].bitcast(F32),
                                            ALU.subtract).then_inc(lo_made, 1)
                    start = AT_FULL
                dve.wait_ge(hi_made, steps_to(g, t))
                nc.vector.tensor_tensor(adj_lo[:, s, start:, :], adj[:, a, start:, :],
                                        adj_hi[:, s, start:, :].bitcast(F32), ALU.subtract).then_inc(lo_made, 1)

            def add_x(g):
                dve.wait_ge(relu_done, g + 1)
                if later(g, 1):
                    dve.wait_ge(z_turned, g)
                nc.vector.tensor_tensor(z_t[:, :, 0:BLOCK],
                                        relu_t[:, :].rearrange("p (b n) -> p b n", b=BLOCKS),
                                        xg[:, :].rearrange("p (b n) -> p b n", b=BLOCKS),
                                        ALU.add).then_inc(z_added, 1)

            def statistics(g):
                dve.wait_ge(z_turned, g + 1)
                for b in range(BLOCKS):
                    ins = nc.vector.bn_stats(stats[:, b, :], z_ps[:, b, :])
                ins.then_inc(stats_done, 1)

            def aggregate(g):
                if later(g, 1):
                    dve.wait_ge(out_ready, g)
                dve.wait_ge(stats_done, g + 1)
                dve.nop(nofuse=True)
                for b in range(BLOCKS):
                    ins = nc.vector.bn_aggr(moments[:, b, :], stats[:, b, :])
                ins.then_inc(moments_done, 1)

            def reciprocal(g):
                dve.wait_ge(std_done, g + 1)
                nc.vector.reciprocal(rstd[:, :], std[:, :]).then_inc(rstd_done, 1)

            def mean_shift(g):
                dve.wait_ge(rstd_done, g + 1)
                nc.vector.scalar_tensor_tensor(out=shift[:, :], in0=moments[:, :, 0], scalar=-1.0,
                                               in1=rstd[:, :], op0=ALU.mult, op1=ALU.mult).then_inc(shift_done, 1)

            def group(g):
                for t in range(TILES):
                    split_lo(g, t)
                    if t == ADD_X_AT:
                        add_x(g - 1)
                    if t == STATS_AT:
                        statistics(g - 1)
                    if t == MOMENTS_AT:
                        aggregate(g - 1)
                    if t == RSTD_AT:
                        reciprocal(g - 1)
                    if t == SHIFT_AT:
                        mean_shift(g - 1)

            nc.vector.memset(eps[:, :], EPS)
            nc.vector.memset(z_t[:, :, :], 0.0).then_inc(pads_ready, 1)
            dve.wait_ge(pads_ready, 1)
            dve.wait_ge(weights_landed, 64)
            add_item_bias(0)
            add_item_bias(1)
            for t in range(TILES):
                split_lo(0, t)
                if t + 2 < TILES:
                    add_item_bias(t + 2)
            group(1)
            with dve.Fori(1, PAIRS) as i:
                group(2 * i)
                group(2 * i + 1)
            add_x(GROUPS - 1)
            statistics(GROUPS - 1)
            aggregate(GROUPS - 1)
            reciprocal(GROUPS - 1)
            mean_shift(GROUPS - 1)


def kernel(x, adj, L0_gnn_item_feat, L0_gnn_W_item, L0_gnn_b_item, L0_gnn_W_user, L0_gnn_b_user):
    import numpy as np
    import concourse.bacc as bacc
    from concourse.bass_utils import run_bass_kernel_spmd

    full = FULL * P
    groups = np.asarray(adj).reshape(GROUPS, GROUP, N_ITEM)
    arrays = {
        "adj_t": np.ascontiguousarray(groups[:, :, :full].reshape(GROUPS, GROUP, FULL, P).transpose(0, 3, 2, 1)),
        "adj_tail": np.ascontiguousarray(groups[:, :, full:].transpose(0, 2, 1)),
        "x_t": np.ascontiguousarray(np.asarray(x).reshape(GROUPS, GROUP, HID).transpose(0, 2, 1)),
        "item_t": np.ascontiguousarray(np.asarray(L0_gnn_item_feat).T),
        "w_item_t": np.ascontiguousarray(np.asarray(L0_gnn_W_item).T),
        "b_item": np.ascontiguousarray(L0_gnn_b_item),
        "w_user_t": np.ascontiguousarray(np.asarray(L0_gnn_W_user).T),
        "b_user": np.ascontiguousarray(L0_gnn_b_user),
    }
    nc = bacc.Bacc("TRN2", target_bir_lowering=False, num_devices=1)
    args = [nc.dram_tensor(n, v.shape, mybir.dt.from_np(v.dtype), kind="ExternalInput").ap() for n, v in arrays.items()]
    out = nc.dram_tensor("out", (GROUPS, P, BLOCKS, HID), F32, kind="ExternalOutput").ap()
    gnn_kernel(nc, *args, out)
    r = run_bass_kernel_spmd(nc, [arrays], core_ids=[0])
    got = r.results[0]["out"]
    return np.ascontiguousarray(got[:, :BLOCK].transpose(0, 2, 1, 3).reshape(N_USER, HID))
```
